# Optimizing a Trainium2 kernel written in Bass

```python
import numpy as np
import jax
import jax.numpy as jnp

def _softmax(x, axis=-1):
    return jax.nn.softmax(x, axis=axis)

def _gelu(x):
    return jax.nn.gelu(x, approximate=True)

def _silu(x):
    return jax.nn.silu(x)

def _sigmoid(x):
    return jax.nn.sigmoid(x)

def _layernorm(x, axis=-1, eps=1e-05):
    m = jnp.mean(x, axis=axis, keepdims=True)
    v = jnp.var(x, axis=axis, keepdims=True)
    return (x - m) / jnp.sqrt(v + eps)

def _scatter_add(tgt, idx, src, axis=0):
    return tgt.at[idx].add(src)

def _segment_sum(src, seg, n):
    return jax.ops.segment_sum(src, seg, n)
kernel_name = 'mk_dlrm_tower_d1_rec_r8_8940a3'

def setup_inputs(seed: int=0):
    np.random.seed(seed)
    _w = jnp.asarray

    def _rec_inputs():
        import jax
        import jax.numpy as jnp
        _tk = jax.random.key(seed)
        ids = jnp.stack([jax.random.randint(jax.random.fold_in(_tk, 200 + f), (512,), 0, v, jnp.int32) for f, v in enumerate([12500, 12500, 1250, 1250, 125000, 12500, 1000, 1250, 1000, 12500, 1250, 1000, 1250, 1000, 1000, 12500, 12500, 1000, 1000, 12500, 1000, 1250, 1250, 12500, 1250, 1000])], axis=1)
        tbl_0 = 0.05 * jax.random.normal(jax.random.fold_in(_tk, 500 + 0), (12500, 128), jnp.float32)
        tbl_1 = 0.05 * jax.random.normal(jax.random.fold_in(_tk, 500 + 1), (12500, 128), jnp.float32)
        tbl_2 = 0.05 * jax.random.normal(jax.random.fold_in(_tk, 500 + 2), (1250, 128), jnp.float32)
        tbl_3 = 0.05 * jax.random.normal(jax.random.fold_in(_tk, 500 + 3), (1250, 128), jnp.float32)
        tbl_4 = 0.05 * jax.random.normal(jax.random.fold_in(_tk, 500 + 4), (125000, 128), jnp.float32)
        tbl_5 = 0.05 * jax.random.normal(jax.random.fold_in(_tk, 500 + 5), (12500, 128), jnp.float32)
        tbl_6 = 0.05 * jax.random.normal(jax.random.fold_in(_tk, 500 + 6), (1000, 128), jnp.float32)
        tbl_7 = 0.05 * jax.random.normal(jax.random.fold_in(_tk, 500 + 7), (1250, 128), jnp.float32)
        tbl_8 = 0.05 * jax.random.normal(jax.random.fold_in(_tk, 500 + 8), (1000, 128), jnp.float32)
        tbl_9 = 0.05 * jax.random.normal(jax.random.fold_in(_tk, 500 + 9), (12500, 128), jnp.float32)
        tbl_10 = 0.05 * jax.random.normal(jax.random.fold_in(_tk, 500 + 10), (1250, 128), jnp.float32)
        tbl_11 = 0.05 * jax.random.normal(jax.random.fold_in(_tk, 500 + 11), (1000, 128), jnp.float32)
        tbl_12 = 0.05 * jax.random.normal(jax.random.fold_in(_tk, 500 + 12), (1250, 128), jnp.float32)
        tbl_13 = 0.05 * jax.random.normal(jax.random.fold_in(_tk, 500 + 13), (1000, 128), jnp.float32)
        tbl_14 = 0.05 * jax.random.normal(jax.random.fold_in(_tk, 500 + 14), (1000, 128), jnp.float32)
        tbl_15 = 0.05 * jax.random.normal(jax.random.fold_in(_tk, 500 + 15), (12500, 128), jnp.float32)
        tbl_16 = 0.05 * jax.random.normal(jax.random.fold_in(_tk, 500 + 16), (12500, 128), jnp.float32)
        tbl_17 = 0.05 * jax.random.normal(jax.random.fold_in(_tk, 500 + 17), (1000, 128), jnp.float32)
        tbl_18 = 0.05 * jax.random.normal(jax.random.fold_in(_tk, 500 + 18), (1000, 128), jnp.float32)
        tbl_19 = 0.05 * jax.random.normal(jax.random.fold_in(_tk, 500 + 19), (12500, 128), jnp.float32)
        tbl_20 = 0.05 * jax.random.normal(jax.random.fold_in(_tk, 500 + 20), (1000, 128), jnp.float32)
        tbl_21 = 0.05 * jax.random.normal(jax.random.fold_in(_tk, 500 + 21), (1250, 128), jnp.float32)
        tbl_22 = 0.05 * jax.random.normal(jax.random.fold_in(_tk, 500 + 22), (1250, 128), jnp.float32)
        tbl_23 = 0.05 * jax.random.normal(jax.random.fold_in(_tk, 500 + 23), (12500, 128), jnp.float32)
        tbl_24 = 0.05 * jax.random.normal(jax.random.fold_in(_tk, 500 + 24), (1250, 128), jnp.float32)
        tbl_25 = 0.05 * jax.random.normal(jax.random.fold_in(_tk, 500 + 25), (1000, 128), jnp.float32)
        _rk = jax.random.fold_in(_tk, 7)
        r_dense_features = -0.000520686 + 1.00062 * jax.random.normal(jax.random.fold_in(_rk, 101), (512, 128), jnp.float32)
        W_top1 = 0.0405887 * jax.random.normal(jax.random.fold_in(_tk, 801), (607, 512), jnp.float32)
        W_top2 = 0.0441942 * jax.random.normal(jax.random.fold_in(_tk, 802), (512, 256), jnp.float32)
        W_top3 = 0.0625 * jax.random.normal(jax.random.fold_in(_tk, 803), (256, 1), jnp.float32)
        b_top1 = jnp.zeros((512,), jnp.float32)
        b_top2 = jnp.zeros((256,), jnp.float32)
        return (r_dense_features, ids, tbl_0, tbl_1, tbl_2, tbl_3, tbl_4, tbl_5, tbl_6, tbl_7, tbl_8, tbl_9, tbl_10, tbl_11, tbl_12, tbl_13, tbl_14, tbl_15, tbl_16, tbl_17, tbl_18, tbl_19, tbl_20, tbl_21, tbl_22, tbl_23, tbl_24, tbl_25, W_top1, b_top1, W_top2, b_top2, W_top3)
    r_dense_features, ids, tbl_0, tbl_1, tbl_2, tbl_3, tbl_4, tbl_5, tbl_6, tbl_7, tbl_8, tbl_9, tbl_10, tbl_11, tbl_12, tbl_13, tbl_14, tbl_15, tbl_16, tbl_17, tbl_18, tbl_19, tbl_20, tbl_21, tbl_22, tbl_23, tbl_24, tbl_25, W_top1, b_top1, W_top2, b_top2, W_top3 = _rec_inputs()

    def _L0_rec_setup():
        import jax, jax.numpy as jnp
        import numpy as np
        NUM_SPARSE = 26
        EMBED_DIM = 128
        BATCH = 2048
        key = jax.random.key(seed)
        k1, k2 = jax.random.split(key)
        dense_features = jax.random.normal(k1, (BATCH, EMBED_DIM), dtype=jnp.float32)
        sparse_features = jax.random.normal(k2, (BATCH, NUM_SPARSE, EMBED_DIM), dtype=jnp.float32)
        return {'dense_features': dense_features, 'sparse_features': sparse_features}
    _L0_rec_all = _L0_rec_setup()
    _L0_rec_in = {k: v for k, v in _L0_rec_all.items() if k in ()}
    del _L0_rec_all
    return {'r_dense_features': r_dense_features, 'ids': ids, 'tbl_0': tbl_0, 'tbl_1': tbl_1, 'tbl_2': tbl_2, 'tbl_3': tbl_3, 'tbl_4': tbl_4, 'tbl_5': tbl_5, 'tbl_6': tbl_6, 'tbl_7': tbl_7, 'tbl_8': tbl_8, 'tbl_9': tbl_9, 'tbl_10': tbl_10, 'tbl_11': tbl_11, 'tbl_12': tbl_12, 'tbl_13': tbl_13, 'tbl_14': tbl_14, 'tbl_15': tbl_15, 'tbl_16': tbl_16, 'tbl_17': tbl_17, 'tbl_18': tbl_18, 'tbl_19': tbl_19, 'tbl_20': tbl_20, 'tbl_21': tbl_21, 'tbl_22': tbl_22, 'tbl_23': tbl_23, 'tbl_24': tbl_24, 'tbl_25': tbl_25, 'W_top1': W_top1, 'b_top1': b_top1, 'W_top2': W_top2, 'b_top2': b_top2, 'W_top3': W_top3}

def reference(r_dense_features, ids, tbl_0, tbl_1, tbl_2, tbl_3, tbl_4, tbl_5, tbl_6, tbl_7, tbl_8, tbl_9, tbl_10, tbl_11, tbl_12, tbl_13, tbl_14, tbl_15, tbl_16, tbl_17, tbl_18, tbl_19, tbl_20, tbl_21, tbl_22, tbl_23, tbl_24, tbl_25, W_top1, b_top1, W_top2, b_top2, W_top3):
    import jax
    import jax.numpy as jnp

    def _L0_rec_ref(dense_features, sparse_features):
        import jax, jax.numpy as jnp
        import numpy as np
        NUM_SPARSE = 26
        EMBED_DIM = 128
        BATCH = 2048
        F = NUM_SPARSE + 1
        combined = jnp.concatenate([dense_features[:, None, :], sparse_features], axis=1)
        interactions = jnp.einsum('bfd,bgd->bfg', combined, combined)
        iu, ju = jnp.triu_indices(F, k=1)
        interactions_flat = interactions[:, iu, ju]
        return jnp.concatenate([dense_features, interactions_flat], axis=1)
    e = jnp.stack([tbl_0[ids[:, 0]], tbl_1[ids[:, 1]], tbl_2[ids[:, 2]], tbl_3[ids[:, 3]], tbl_4[ids[:, 4]], tbl_5[ids[:, 5]], tbl_6[ids[:, 6]], tbl_7[ids[:, 7]], tbl_8[ids[:, 8]], tbl_9[ids[:, 9]], tbl_10[ids[:, 10]], tbl_11[ids[:, 11]], tbl_12[ids[:, 12]], tbl_13[ids[:, 13]], tbl_14[ids[:, 14]], tbl_15[ids[:, 15]], tbl_16[ids[:, 16]], tbl_17[ids[:, 17]], tbl_18[ids[:, 18]], tbl_19[ids[:, 19]], tbl_20[ids[:, 20]], tbl_21[ids[:, 21]], tbl_22[ids[:, 22]], tbl_23[ids[:, 23]], tbl_24[ids[:, 24]], tbl_25[ids[:, 25]]], axis=1)
    z = _L0_rec_ref(r_dense_features, e)
    z = z.reshape(z.shape[0], -1)
    h = jnp.concatenate([z, r_dense_features], axis=1)
    h = jnp.maximum(h @ W_top1 + b_top1, 0.0)
    h = jnp.maximum(h @ W_top2 + b_top2, 0.0)
    y = h @ W_top3
    return y

_drawn_inputs = setup_inputs


def setup_inputs(seed=0):
    import zlib

    import numpy as np

    out = dict(_drawn_inputs(seed))
    spreads = {'b_top1': (0.0, 0.1), 'b_top2': (0.0, 0.1)}
    factors = {}
    for name, (base, spread) in spreads.items():
        noise = np.random.default_rng([zlib.crc32(name.encode()), seed]).standard_normal(out[name].shape)
        drawn = base * np.exp(spread * noise) if base else spread * noise
        out[name] = jnp.asarray(drawn.astype(out[name].dtype))
    for name, factor in factors.items():
        out[name] = (out[name] * factor).astype(out[name].dtype)
    return out
```

```python
import concourse.bass as bass
from concourse import mybir
from concourse.alu_op_type import AluOpType
from contextlib import ExitStack

fp32 = mybir.dt.float32
i32 = mybir.dt.int32
ACT = mybir.ActivationFunctionType

BATCH, D, FIELDS = 512, 128, 26
NV = FIELDS + 1
TB = 128
TILES = BATCH // TB
N1, N2 = 512, 256
C1, C2 = N1 // 128, N2 // 128
QUADS, Q = 4, 32
SLOTS = NV - 1
ZC = -(-SLOTS // QUADS)
GRP = 4
GROUPS = -(-NV // GRP)
VPAD = 32


def members(g):
    return range(g * GRP, min((g + 1) * GRP, NV))


def pair_row(i):
    return D + i * (NV - 1) - i * (i - 1) // 2


def chunk_rows(c):
    return Q * min(QUADS, SLOTS - QUADS * c)


def dlrm_tower(nc, dense, ids, tables, w1, b1, w2, b2, w3, out):
    with ExitStack() as ctx:
        def sb(name, shape, dt=fp32):
            return ctx.enter_context(nc.sbuf_tensor(name, shape, dt))

        def pb(name, shape):
            return ctx.enter_context(nc.psum_tensor(name, shape, fp32))

        def sem(name):
            return ctx.enter_context(nc.semaphore(name))

        idx = sb("idx", [TB, TILES, FIELDS], i32)
        rows = sb("rows", [TB, NV, D])
        vecT = sb("vecT", [D, TB, VPAD])
        pairs = sb("pairs", [128, ZC, TB])
        ident = sb("ident", [128, 128])
        w1d = sb("w1d", [D, N1])
        w1e = sb("w1e", [D, N1])
        w1z = sb("w1z", [128, ZC, N1])
        w2s = sb("w2s", [128, C1, N2])
        w3s = sb("w3s", [128, C2])
        b1s = sb("b1s", [128, C1])
        b2s = sb("b2s", [128, C2])
        h1 = sb("h1", [128, C1, TB])
        h2 = sb("h2", [128, C2, TB])
        y = sb("y", [1, BATCH])

        turned = [pb(f"turned{k}", [128, GRP, TB]) for k in range(2)]
        gram = pb("gram", [128, TB // QUADS, Q])
        h1p = pb("h1p", [128, C1, TB])
        h2p = pb("h2p", [128, C2, TB])
        yp = pb("yp", [1, TB])

        ids_in = sem("ids_in")
        dense_in = sem("dense_in")
        w1z_in = sem("w1z_in")
        w1d_in = sem("w1d_in")
        small_in = sem("small_in")
        gathered = [sem(f"gathered{g}") for g in range(GROUPS)]
        ident_zero = sem("ident_zero")
        ident_ready = sem("ident_ready")
        w1z_zero = sem("w1z_zero")
        pairs_zero = sem("pairs_zero")
        w1d_ready = sem("w1d_ready")
        turn_done = sem("turn_done")
        vec_dve = sem("vec_dve")
        vec_act = sem("vec_act")
        gram_done = sem("gram_done")
        pairs_dve = sem("pairs_dve")
        pairs_act = sem("pairs_act")
        h1_done = sem("h1_done")
        h1_ready = sem("h1_ready")
        h2_done = sem("h2_done")
        h2_ready = sem("h2_ready")
        y_done = sem("y_done")
        y_ready = sem("y_ready")
        stored = sem("stored")
        block = ctx.enter_context(nc.Block())

        EVEN = len(range(0, GROUPS, 2))
        ODD = GROUPS - EVEN

        @block.sync
        def _(sp):
            sp.dma_start(idx[:, :, :], ids.rearrange("(t p) f -> p t f", p=TB)).then_inc(ids_in, 16)
            sp.dma_start(rows[:, 0, :], dense[0:TB, :]).then_inc(dense_in, 16)
            sp.dma_start(w1d[:, :], w1[0:D, :]).then_inc(w1d_in, 16)
            sp.dma_start(w1e[:, :], w1[w1.shape[0] - D:, :]).then_inc(w1d_in, 16)
            sp.wait_ge(w1z_zero, 1)
            for i in range(SLOTS):
                p = Q * (i % QUADS)
                n = NV - 1 - i
                sp.dma_start(w1z[p + i + 1:p + NV, i // QUADS, :],
                             w1[pair_row(i):pair_row(i) + n, :]).then_inc(w1z_in, 16)
            sp.dma_start(w2s[:, :, :], w2.rearrange("(c p) n -> p c n", p=128)).then_inc(small_in, 16)
            sp.dma_start(w3s[:, :], w3).then_inc(small_in, 16)
            sp.dma_start(b1s[:, :], b1).then_inc(small_in, 16)
            sp.dma_start(b2s[:, :], b2).then_inc(small_in, 16)
            with sp.Fori(1, TILES) as t:
                sp.wait_ge(turn_done, t * GROUPS - (GROUPS - 1))
                sp.dma_start(rows[:, 0, :], dense[bass.ds(t * TB, TB), :]).then_inc(dense_in, 16)
            sp.wait_ge(y_ready, TILES)
            sp.dma_start(out, y[:, :]).then_inc(stored, 16)
            sp.wait_ge(stored, 16)

        @block.gpsimd
        def _(pool):
            nc.gpsimd.memset(ident[:, :], 0.0).then_inc(ident_zero, 1)
            pool.wait_ge(ident_zero, 1)
            nc.gpsimd.affine_select(out=ident[:, :], in_=ident[:, :], compare_op=AluOpType.not_equal, fill=1.0,
                                    base=0, pattern=[[-1, 128]], channel_multiplier=1).then_inc(ident_ready, 1)
            pool.wait_ge(ids_in, 16)
            for t in range(TILES):
                for g in range(GROUPS):
                    if t > 0:
                        pool.wait_ge(turn_done, (t - 1) * GROUPS + g + 1)
                    for v in members(g):
                        if v == 0:
                            continue
                        pool.indirect_dma_start(rows[:, v, :], None, tables[v - 1][:, :],
                                                bass.IndirectOffsetOnAxis(ap=idx[:, t, v - 1:v], axis=0)
                                                ).then_inc(gathered[g], 16)

        @block.tensor
        def _(pe):
            def wait_bank(t, g, peeled):
                done, k = (vec_dve, EVEN) if g % 2 == 0 else (vec_act, ODD)
                n = t * k + g // 2
                if not (peeled and g < 2):
                    pe.wait_ge(done, n)

            def turn_tile(t, peeled=False):
                for g in range(GROUPS):
                    n = len([v for v in members(g) if v > 0])
                    pe.wait_ge(gathered[g], t * (16 * n) + 16 * n)
                    if g == 0:
                        pe.wait_ge(dense_in, t * 16 + 16)
                    wait_bank(t, g, peeled)
                    for v in members(g):
                        last = nc.tensor.transpose(turned[g % 2][:, v - g * GRP, :], rows[:, v, :], ident[:, :])
                    last.then_inc(turn_done, 1)

            def gram_tile(t, peeled=False):
                pe.wait_ge(vec_dve, t * EVEN + EVEN)
                pe.wait_ge(vec_act, t * ODD + ODD)
                for k in range(TB // QUADS):
                    for q in range(QUADS):
                        v = vecT[:, q * Q + k, :]
                        last = nc.tensor.matmul(gram[q * Q:q * Q + NV, k, 0:SLOTS], v[:, 0:NV], v[:, 0:SLOTS],
                                                start=True, stop=True)
                last.then_inc(gram_done, 1)

            def mlp_tile(t, peeled=False):
                for n in range(C1):
                    ns = slice(n * 128, (n + 1) * 128)
                    if n == 0 and peeled:
                        pe.wait_ge(w1d_ready, 1)
                    nc.tensor.matmul(h1p[:, n, :], w1d[:, ns], vecT[:, :, 0], start=True, stop=False)
                    if n == 0:
                        pe.wait_ge(pairs_dve, t + 1)
                        pe.wait_ge(pairs_act, t + 1)
                        if peeled:
                            pe.wait_ge(w1z_in, 16 * SLOTS)
                    for c in range(ZC):
                        k = chunk_rows(c)
                        last = nc.tensor.matmul(h1p[:, n, :], w1z[0:k, c, ns], pairs[0:k, c, :],
                                                start=False, stop=(c == ZC - 1))
                last.then_inc(h1_done, 1)

            def mlp2_tile(t, peeled=False):
                pe.wait_ge(h1_ready, t + 1)
                for m in range(C2):
                    for n in range(C1):
                        last = nc.tensor.matmul(h2p[:, m, :], w2s[:, n, m * 128:(m + 1) * 128], h1[:, n, :],
                                                start=(n == 0), stop=(n == C1 - 1))
                last.then_inc(h2_done, 1)
                pe.wait_ge(h2_ready, t + 1)
                for m in range(C2):
                    last = nc.tensor.matmul(yp[:, :], w3s[:, m:m + 1], h2[:, m, :],
                                            start=(m == 0), stop=(m == C2 - 1))
                last.then_inc(y_done, 1)

            pe.wait_ge(ident_ready, 1)
            turn_tile(0, True)
            gram_tile(0)
            mlp_tile(0, True)
            pe.wait_ge(small_in, 64)
            mlp2_tile(0)
            with pe.Fori(1, TILES) as t:
                turn_tile(t)
                gram_tile(t)
                mlp_tile(t)
                mlp2_tile(t)

        def pairs_copy(copy, s):
            for jm in range(QUADS):
                n = len(range(jm, SLOTS, QUADS))
                last = copy(pairs[jm * Q:jm * Q + NV, 0:n, s * Q:(s + 1) * Q],
                            gram[s * Q:s * Q + NV, :, jm:jm + (n - 1) * QUADS + 1:QUADS].rearrange("p k c -> p c k"))
            return last

        def vec_copy(copy, g):
            n = len(members(g))
            return copy(vecT[:, :, g * GRP:g * GRP + n].rearrange("p b v -> p v b"), turned[g % 2][:, 0:n, :])

        @block.vector
        def _(dve):
            nc.vector.memset(w1z[:, :, :], 0.0).then_inc(w1z_zero, 1)
            nc.vector.memset(pairs[:, :, :], 0.0).then_inc(pairs_zero, 1)
            dve.wait_ge(w1d_in, 32)
            nc.vector.tensor_tensor(w1d[:, :], w1d[:, :], w1e[:, :], AluOpType.add).then_inc(w1d_ready, 1)
            dve.wait_ge(pairs_zero, 1)

            def tile(t, peeled=False):
                for g in range(0, GROUPS, 2):
                    dve.wait_ge(turn_done, t * GROUPS + g + 1)
                    vec_copy(nc.vector.tensor_copy, g).then_inc(vec_dve, 1)
                dve.wait_ge(gram_done, t + 1)
                pairs_copy(nc.vector.tensor_copy, 0)
                pairs_copy(nc.vector.tensor_copy, 1).then_inc(pairs_dve, 1)
                dve.wait_ge(h2_done, t + 1)
                for m in range(C2):
                    last = nc.vector.tensor_scalar(h2[:, m, :], h2p[:, m, :], b2s[:, m:m + 1], 0.0,
                                                   AluOpType.add, AluOpType.max)
                last.then_inc(h2_ready, 1)
                dve.wait_ge(y_done, t + 1)
                nc.vector.tensor_copy(y[:, bass.ds(t * TB, TB)], yp[:, :]).then_inc(y_ready, 1)

            tile(0)
            with dve.Fori(1, TILES) as t:
                tile(t)

        @block.scalar
        def _(act):
            act.wait_ge(pairs_zero, 1)

            def tile(t, peeled=False):
                for g in range(1, GROUPS, 2):
                    act.wait_ge(turn_done, t * GROUPS + g + 1)
                    vec_copy(nc.scalar.copy, g).then_inc(vec_act, 1)
                act.wait_ge(gram_done, t + 1)
                pairs_copy(nc.scalar.copy, 2)
                pairs_copy(nc.scalar.copy, 3).then_inc(pairs_act, 1)
                act.wait_ge(h1_done, t + 1)
                for n in range(C1):
                    last = nc.scalar.activation(h1[:, n, :], h1p[:, n, :], ACT.Relu, bias=b1s[:, n:n + 1])
                last.then_inc(h1_ready, 1)

            act.wait_ge(small_in, 64)
            tile(0)
            with act.Fori(1, TILES) as t:
                tile(t)


INPUTS = (["r_dense_features", "ids"] + [f"tbl_{f}" for f in range(FIELDS)]
          + ["W_top1", "b_top1", "W_top2", "b_top2", "W_top3"])


def kernel(**inputs):
    import numpy as np
    import concourse.bacc as bacc
    from concourse import mybir
    from concourse.bass_utils import run_bass_kernel_spmd as run

    nc = bacc.Bacc("TRN2", target_bir_lowering=False, num_devices=1)
    arrays, ap = {}, {}
    for name in INPUTS:
        a = np.asarray(inputs[name])
        if name in ("b_top1", "b_top2", "W_top3"):
            a = a.reshape(-1, 128).T
        a = np.ascontiguousarray(a)
        arrays["in_" + name] = a
        ap[name] = nc.dram_tensor("in_" + name, a.shape, mybir.dt.from_np(a.dtype), kind="ExternalInput").ap()
    out = nc.dram_tensor("out_y", (1, BATCH), mybir.dt.float32, kind="ExternalOutput").ap()
    dlrm_tower(nc, ap["r_dense_features"], ap["ids"], [ap[f"tbl_{f}"] for f in range(FIELDS)],
               ap["W_top1"], ap["b_top1"], ap["W_top2"], ap["b_top2"], ap["W_top3"], out)
    r = run(nc, [arrays], core_ids=[0])
    return r.results[0]["out_y"].reshape(BATCH, 1)
```

```python
import concourse.bass as bass
from concourse import mybir
from concourse.alu_op_type import AluOpType
from contextlib import ExitStack

fp32 = mybir.dt.float32
fp32r = mybir.dt.float32r
i32 = mybir.dt.int32
ACT = mybir.ActivationFunctionType

BATCH, D, FIELDS = 512, 128, 26
NV = FIELDS + 1
TB = 128
TILES = BATCH // TB
N1, N2 = 512, 256
C1 = N1 // 128
QUADS, Q = 4, 32
SLOTS = NV - 1
ZC = -(-SLOTS // QUADS)
ZHALF = (ZC + 1) // 2
BIAS_ROW = Q * (SLOTS - QUADS * (ZC - 1))
GRP = 4
FOUR = Q * (QUADS - 1) + NV
VPAD = Q
SHARE = 125
PICKED = [11, 13, 14, 17, 18, 20, 25]
NP = len(PICKED)
ACT_LOTS = 2
BATCH_K = 8
GRAMS = TB // QUADS // BATCH_K


def runs(vectors):
    out = []
    for v in vectors:
        r = out[-1] if out else []
        if r and len(r) < GRP and (len(r) == 1 or v - r[-1] == r[1] - r[0]):
            r.append(v)
        else:
            out.append([v])
    return out


def span(run):
    return slice(run[0], run[-1] + 1, run[1] - run[0] if len(run) > 1 else 1)


GROUPS = runs([v for v in range(1, NV) if v - 1 not in PICKED])
NG = len(GROUPS)
EVEN, ODD = len(GROUPS[0::2]), len(GROUPS[1::2])
AFTER_PRODUCTS, AFTER_LAYER1, AFTER_HIDDEN = range(0, 2), range(2, 4), range(4, NG)
WHOLE = [0] + [f + 1 for f in PICKED]
WHOLE_RUNS = runs(WHOLE)
GATHERED = sum(len(group) for group in GROUPS)
RING = 28
RING_OF = {v: n for n, v in enumerate(v for group in GROUPS for v in group)}


def place(t, v):
    return (t * GATHERED + RING_OF[v]) % RING


def last_turn(t, v):
    n = t * GATHERED + RING_OF[v] - RING
    if n < 0:
        return 0
    g = [g for g, group in enumerate(GROUPS) for _ in group][n % GATHERED]
    return n // GATHERED * NG + g + 1


def pair_row(i):
    return D + i * (NV - 1) - i * (i - 1) // 2


def chunk_rows(c):
    return BIAS_ROW + 1 if c == ZC - 1 else 128


W1_PIECES = [range(c, min(c + 2, ZC)) for c in range(0, ZC, 2)]


def slots_of(n):
    return range(QUADS * W1_PIECES[n][0], min(QUADS * (W1_PIECES[n][-1] + 1), SLOTS))


def dlrm_tower(nc, dense, ids, ids_by_field, tables, w1, b1, w2, b2, w3, out):
    LOTS = tables[PICKED[0]].shape[0] // SHARE
    DVE_LOTS = LOTS - ACT_LOTS
    for f in PICKED:
        assert LOTS * SHARE == tables[f].shape[0]

    with ExitStack() as ctx:
        def sb(name, shape, dt=fp32):
            return ctx.enter_context(nc.sbuf_tensor(name, shape, dt))

        def pb(name, shape):
            return ctx.enter_context(nc.psum_tensor(name, shape, fp32))

        def sem(name):
            return ctx.enter_context(nc.semaphore(name))

        idx = sb("idx", [TB, TILES, FIELDS], i32)
        idb = sb("idb", [128, 2, BATCH], i32)
        rowid = sb("rowid", [128, LOTS])
        minus_rowid = sb("minus_rowid", [128, LOTS])
        distance = sb("distance", [SHARE, ACT_LOTS, BATCH])
        raw = sb("raw", [SHARE, 2, LOTS, D])
        hi = sb("hi", [SHARE, 2, LOTS, D], fp32r)
        lo = sb("lo", [SHARE, 2, LOTS, D], fp32r)
        onehot = sb("onehot", [SHARE, 2, LOTS, BATCH], fp32r)
        whole = sb("whole", [D, 1 + NP, BATCH])
        drows = sb("drows", [TB, TILES, D])
        rows = sb("rows", [TB, RING, D])
        vecT = sb("vecT", [D, Q, QUADS, VPAD])
        dhi = sb("dhi", [D, TB], fp32r)
        dlo = sb("dlo", [D, TB], fp32r)
        pairs = sb("pairs", [128, ZC, TB])
        phi = sb("phi", [128, ZC, TB], fp32r)
        plo = sb("plo", [128, ZC, TB], fp32r)
        ident = sb("ident", [128, 128])
        zeros = sb("zeros", [128, N1])
        w1d = sb("w1d", [D, 2, N1])
        wdhi = sb("wdhi", [D, N1], fp32r)
        wdlo = sb("wdlo", [D, N1], fp32r)
        w1z = sb("w1z", [128, ZC, N1])
        wzhi = sb("wzhi", [128, ZC, N1], fp32r)
        wzlo = sb("wzlo", [128, ZC, N1], fp32r)
        w2s = sb("w2s", [128, C1, N2])
        b2s = sb("b2s", [128, N2])
        w3s = sb("w3s", [128, N2])
        h1 = sb("h1", [TB, C1, 128])
        h1T = sb("h1T", [128, C1, TB])
        h2 = sb("h2", [TB, N2])
        weighted = sb("weighted", [TB, N2])
        y = sb("y", [TB, TILES])

        turned = [pb(f"turned{k}", [128, GRP, TB]) for k in range(2)]
        gram = [pb(f"gram{k}", [128, BATCH_K, 128]) for k in range(2)]
        picked_acc = [gram[k][:, 0:GRP, :].rearrange("p a b -> p (a b)") for k in range(2)]
        h1p = pb("h1p", [TB, N1])
        h2p = h1p[:, 0:N2]
        h1Tp = pb("h1Tp", [128, C1, TB])

        ids_in = sem("ids_in")
        idb_in = [sem(f"idb_in{k}") for k in range(2)]
        table_in = [sem(f"table_in{k}") for k in range(2)]
        dense_in = sem("dense_in")
        zeros_ready = sem("zeros_ready")
        w1z_zero = [sem(f"w1z_zero{n}") for n in range(len(W1_PIECES))]
        w1z_in = [sem(f"w1z_in{n}") for n in range(len(W1_PIECES))]
        w1d_in = sem("w1d_in")
        small_in = sem("small_in")
        gathered = [[sem(f"gathered{k}_{g}") for g in range(NG)] for k in range(2)]
        ident_zero = sem("ident_zero")
        ident_ready = sem("ident_ready")
        rowid_ready = sem("rowid_ready")
        pads_zero = sem("pads_zero")
        w1d_added = sem("w1d_added")
        w1_hi = sem("w1_hi")
        w1_lo = sem("w1_lo")
        minus_ready = sem("minus_ready")
        distance_ready = sem("distance_ready")
        hi_ready = sem("hi_ready")
        lo_ready = sem("lo_ready")
        marked_dve = sem("marked_dve")
        marked_act = sem("marked_act")
        picked = sem("picked")
        dense_turned = sem("dense_turned")
        dense_kept = sem("dense_kept")
        kept = sem("kept")
        turn_done = sem("turn_done")
        vec_dve = sem("vec_dve")
        vec_act = sem("vec_act")
        spread = sem("spread")
        dhi_ready = sem("dhi_ready")
        dlo_ready = sem("dlo_ready")
        gram_done = sem("gram_done")
        pairs_dve = sem("pairs_dve")
        pairs_act = sem("pairs_act")
        phi_ready = sem("phi_ready")
        plo_ready = sem("plo_ready")
        h1_done = sem("h1_done")
        h1_ready = sem("h1_ready")
        h1T_done = sem("h1T_done")
        h1T_ready = sem("h1T_ready")
        h2_done = sem("h2_done")
        h2_ready = sem("h2_ready")
        y_ready = sem("y_ready")
        stored = sem("stored")
        block = ctx.enter_context(nc.Block())

        def parts(c):
            return slice(c[0], c[-1] + 1)

        @block.sync
        def _(sp):
            def load_table(m):
                f, k = PICKED[m], m % 2
                if m >= 2:
                    sp.wait_ge(lo_ready, m - 1)
                src = tables[f].rearrange("(p c) d -> p c d", c=LOTS)
                cut = SHARE - SHARE % 15
                for a, b in ((0, cut), (cut, SHARE)):
                    sp.dma_start(raw[a:b, k, :, :], src[a:b, :, :]).then_inc(table_in[k], 16)

            def load_ids(m):
                if m >= 2:
                    sp.wait_ge(marked_dve, DVE_LOTS * (m - 1))
                    sp.wait_ge(marked_act, ACT_LOTS * (m - 1))
                f = PICKED[m]
                sp.dma_start(idb[:, m % 2, :],
                             ids_by_field[f:f + 1, :].to_broadcast([128, BATCH])).then_inc(idb_in[m % 2], 16)

            def clear_w1z(n):
                c = parts(W1_PIECES[n])
                sp.dma_start(w1z[:, c, :], zeros[:, :].unsqueeze(1).to_broadcast([128, c.stop - c.start, N1])
                             ).then_inc(w1z_zero[n], 16)

            def load_w1z(n):
                sp.wait_ge(w1z_zero[n], 16)
                for i in slots_of(n):
                    p = Q * (i % QUADS)
                    sp.dma_start(w1z[p + i + 1:p + NV, i // QUADS, :],
                                 w1[pair_row(i):pair_row(i) + NV - 1 - i, :]).then_inc(w1z_in[n], 16)
                if n == len(W1_PIECES) - 1:
                    sp.dma_start(w1z[BIAS_ROW:BIAS_ROW + 1, ZC - 1, :], b1).then_inc(w1z_in[n], 16)

            load_ids(0)
            sp.dma_start(idx[:, :, :], ids.rearrange("(t p) f -> p t f", p=TB)).then_inc(ids_in, 16)
            load_table(0)
            load_ids(1)
            load_table(1)
            sp.dma_start(drows[:, :, :], dense.rearrange("(t p) d -> p t d", p=TB)).then_inc(dense_in, 16)
            load_table(2)
            load_ids(2)
            sp.wait_ge(zeros_ready, 1)
            clear_w1z(0)
            clear_w1z(1)
            load_table(3)
            load_ids(3)
            sp.dma_start(w1d[:, 0, :], w1[0:D, :]).then_inc(w1d_in, 16)
            sp.dma_start(w1d[:, 1, :], w1[w1.shape[0] - D:, :]).then_inc(w1d_in, 16)
            clear_w1z(2)
            clear_w1z(3)
            for m in range(4, NP):
                load_table(m)
                load_ids(m)
                load_w1z(m - 4)
            for n in range(NP - 4, len(W1_PIECES)):
                load_w1z(n)
            sp.dma_start(w2s[:, :, :], w2.rearrange("(c p) n -> p c n", p=128)).then_inc(small_in, 16)
            sp.dma_start(b2s[:, :], b2.to_broadcast([128, N2])).then_inc(small_in, 16)
            sp.dma_start(w3s[:, :], w3.to_broadcast([128, N2])).then_inc(small_in, 16)
            sp.wait_ge(y_ready, TILES)
            sp.dma_start(out, y[:, :]).then_inc(stored, 16)
            sp.wait_ge(stored, 16)

        @block.gpsimd
        def _(pool):
            nc.gpsimd.iota(rowid[:, :], pattern=[[1, LOTS]], base=0, channel_multiplier=LOTS,
                           allow_small_or_imprecise_dtypes=True).then_inc(rowid_ready, 1)
            nc.gpsimd.memset(ident[:, :], 0.0).then_inc(ident_zero, 1)
            pool.wait_ge(ident_zero, 1)
            nc.gpsimd.affine_select(out=ident[:, :], in_=ident[:, :], compare_op=AluOpType.not_equal, fill=1.0,
                                    base=0, pattern=[[-1, 128]], channel_multiplier=1).then_inc(ident_ready, 1)
            nc.gpsimd.memset(zeros[:, :], 0.0).then_inc(zeros_ready, 1)
            pool.wait_ge(ids_in, 16)
            for t in range(TILES):
                for g, group in enumerate(GROUPS):
                    for v in group:
                        if last_turn(t, v):
                            pool.wait_ge(turn_done, last_turn(t, v))
                        pool.indirect_dma_start(rows[:, place(t, v), :], None, tables[v - 1][:, :],
                                                bass.IndirectOffsetOnAxis(ap=idx[:, t, v - 1:v], axis=0)
                                                ).then_inc(gathered[t % 2][g], 16)

        @block.tensor
        def _(pe):
            def pick(m):
                k = m % 2
                if m >= 2:
                    pe.wait_ge(kept, m - 1)
                pe.wait_ge(hi_ready, m + 1)
                for c in range(LOTS):
                    if c < DVE_LOTS:
                        pe.wait_ge(marked_dve, DVE_LOTS * m + c + 1)
                    else:
                        pe.wait_ge(marked_act, ACT_LOTS * m + c - DVE_LOTS + 1)
                    nc.tensor.matmul(picked_acc[k], hi[:, k, c, :], onehot[:, k, c, :], start=(c == 0), stop=False)
                pe.wait_ge(lo_ready, m + 1)
                for c in range(LOTS):
                    last = nc.tensor.matmul(picked_acc[k], lo[:, k, c, :], onehot[:, k, c, :],
                                            start=False, stop=(c == LOTS - 1))
                last.then_inc(picked, 1)

            def turn(t, g, free=True):
                group = GROUPS[g]
                pe.wait_ge(gathered[t % 2][g], (t // 2 + 1) * 16 * len(group))
                if free:
                    if g % 2 == 0:
                        pe.wait_ge(vec_dve, t * EVEN + g // 2)
                    else:
                        pe.wait_ge(vec_act, t * ODD + g // 2)
                for n, v in enumerate(group):
                    last = nc.tensor.transpose(turned[g % 2][:, n, :], rows[:, place(t, v), :], ident[:, :])
                last.then_inc(turn_done, 1)

            def products(t):
                pe.wait_ge(vec_dve, t * EVEN + EVEN)
                pe.wait_ge(vec_act, t * ODD + ODD)
                pe.wait_ge(spread, t + 1)
                for n in range(GRAMS):
                    if n >= 2:
                        pe.wait_ge(pairs_dve, t * GRAMS + n - 1)
                        pe.wait_ge(pairs_act, t * GRAMS + n - 1)
                    for k in range(BATCH_K):
                        four = vecT[:, n * BATCH_K + k, :, :]
                        last = nc.tensor.matmul(gram[n % 2][0:FOUR, k, 0:QUADS * SLOTS],
                                                four.rearrange("p s v -> p (s v)")[:, 0:FOUR],
                                                four[:, :, 0:SLOTS], start=True, stop=True)
                    last.then_inc(gram_done, 1)

            def layer1(t):
                pe.wait_ge(dhi_ready, t + 1)
                pe.wait_ge(dlo_ready, t + 1)
                nc.tensor.matmul(h1p[:, :], dhi[:, :], wdhi[:, :], start=True, stop=False)
                nc.tensor.matmul(h1p[:, :], dhi[:, :], wdlo[:, :], start=False, stop=False)
                nc.tensor.matmul(h1p[:, :], dlo[:, :], wdhi[:, :], start=False, stop=False)
                for half, chunks in enumerate((range(ZHALF), range(ZHALF, ZC))):
                    pe.wait_ge(phi_ready, t * 2 + half + 1)
                    for c in chunks:
                        k = chunk_rows(c)
                        nc.tensor.matmul(h1p[:, :], phi[0:k, c, :], wzhi[0:k, c, :], start=False, stop=False)
                        nc.tensor.matmul(h1p[:, :], phi[0:k, c, :], wzlo[0:k, c, :], start=False, stop=False)
                    pe.wait_ge(plo_ready, t * 2 + half + 1)
                    for c in chunks:
                        k = chunk_rows(c)
                        last = nc.tensor.matmul(h1p[:, :], plo[0:k, c, :], wzhi[0:k, c, :],
                                                start=False, stop=(c == ZC - 1))
                last.then_inc(h1_done, 1)

            def turn_hidden(t):
                for n in range(C1):
                    if n % (C1 // 2) == 0:
                        pe.wait_ge(h1_ready, t * 2 + n // (C1 // 2) + 1)
                    last = nc.tensor.transpose(h1Tp[:, n, :], h1[:, n, :], ident[:, :])
                last.then_inc(h1T_done, 1)

            def layer2(t):
                pe.wait_ge(h1T_ready, t + 1)
                for n in range(C1):
                    last = nc.tensor.matmul(h2p, h1T[:, n, :], w2s[:, n, :], start=(n == 0), stop=(n == C1 - 1))
                last.then_inc(h2_done, 1)

            pe.wait_ge(ident_ready, 1)
            for m in range(NP):
                pick(m)
                if m == 0:
                    pe.wait_ge(dense_in, 16)
                    for t in range(TILES):
                        last = nc.tensor.transpose(turned[1][:, t, :], drows[:, t, :], ident[:, :])
                    last.then_inc(dense_turned, 1)
                elif m <= NG:
                    if m == 2:
                        pe.wait_ge(dense_kept, 1)
                    turn(0, m - 1, free=(m > 2))
            for g in range(NP - 1, NG):
                turn(0, g)
            pe.wait_ge(w1_hi, 1 + len(W1_PIECES))
            pe.wait_ge(w1_lo, 1 + len(W1_PIECES))
            pe.wait_ge(small_in, 48)
            for t in range(TILES):
                products(t)
                if t + 1 < TILES:
                    for g in AFTER_PRODUCTS:
                        turn(t + 1, g)
                layer1(t)
                if t + 1 < TILES:
                    for g in AFTER_LAYER1:
                        turn(t + 1, g)
                turn_hidden(t)
                if t + 1 < TILES:
                    for g in AFTER_HIDDEN:
                        turn(t + 1, g)
                layer2(t)

        def pairs_copy(copy, s, n):
            for jm in range(QUADS):
                slots = len(range(jm, SLOTS, QUADS))
                a = s * SLOTS + jm
                last = copy(pairs[jm * Q:jm * Q + NV, 0:slots, s * Q + n * BATCH_K:s * Q + (n + 1) * BATCH_K],
                            gram[n % 2][s * Q:s * Q + NV, :, a:a + (slots - 1) * QUADS + 1:QUADS]
                            .rearrange("p k c -> p c k"))
            return last

        def vec_copy(copy, g):
            return copy(vecT[:, :, :, span(GROUPS[g])].rearrange("p k s v -> p v s k"),
                        turned[g % 2][:, 0:len(GROUPS[g]), :].rearrange("p v (s k) -> p v s k", k=Q))

        @block.vector
        def _(dve):
            def rest(out, whole_value, upper):
                return nc.vector.tensor_tensor(out, whole_value, upper.bitcast(fp32), AluOpType.subtract)

            def mark(m):
                k = m % 2
                dve.wait_ge(idb_in[k], 16 * (m // 2 + 1))
                if m >= 2:
                    dve.wait_ge(picked, m - 1)
                for c in range(DVE_LOTS):
                    nc.vector.tensor_scalar(onehot[:, k, c, :], idb[0:SHARE, k, :], rowid[0:SHARE, c:c + 1],
                                            None, AluOpType.is_equal).then_inc(marked_dve, 1)
                dve.wait_ge(hi_ready, m + 1)
                rest(lo[:, k, :, :], raw[:, k, :, :], hi[:, k, :, :]).then_inc(lo_ready, 1)

            def w1_rest(n):
                c = parts(W1_PIECES[n])
                dve.wait_ge(w1_hi, n + 1)
                rest(wzlo[:, c, :], w1z[:, c, :], wzhi[:, c, :]).then_inc(w1_lo, 1)
                if n == len(W1_PIECES) - 1:
                    dve.wait_ge(w1_hi, n + 2)
                    rest(wdlo[:, :], w1d[:, 0, :], wdhi[:, :]).then_inc(w1_lo, 1)

            def group_copies(t, groups):
                for g in groups:
                    if g % 2 == 0:
                        dve.wait_ge(turn_done, t * NG + g + 1)
                        vec_copy(nc.vector.tensor_copy, g).then_inc(vec_dve, 1)

            def pair_copies(t):
                for n in range(GRAMS):
                    dve.wait_ge(gram_done, t * GRAMS + n + 1)
                    pairs_copy(nc.vector.tensor_copy, 0, n)
                    pairs_copy(nc.vector.tensor_copy, 1, n).then_inc(pairs_dve, 1)
                for half, c in enumerate((slice(0, ZHALF), slice(ZHALF, ZC))):
                    dve.wait_ge(phi_ready, t * 2 + half + 1)
                    rest(plo[:, c, :], pairs[:, c, :], phi[:, c, :]).then_inc(plo_ready, 1)

            def dense_rest(t):
                dve.wait_ge(dhi_ready, t + 1)
                rest(dlo[:, :], whole[:, 0, bass.ds(t * TB, TB)], dhi[:, :]).then_inc(dlo_ready, 1)

            def output(t):
                dve.wait_ge(h2_done, t + 1)
                nc.vector.tensor_tensor(h2[:, :], h2p, b2s[:, :], AluOpType.add).then_inc(h2_ready, 1)
                dve.wait_ge(h2_ready, t + 1)
                nc.vector.scalar_tensor_tensor(weighted[:, :], h2[:, :], 0.0, w3s[:, :], AluOpType.max, AluOpType.mult,
                                               accum_out=y[:, bass.ds(t, 1)]).then_inc(y_ready, 1)

            dve.wait_ge(rowid_ready, 1)
            mark(0)
            nc.vector.memset(vecT[:, :, :, NV:VPAD], 0.0)
            nc.vector.memset(pairs[:, :, :], 0.0).then_inc(pads_zero, 1)
            dve.wait_ge(pads_zero, 1)
            nc.vector.memset(pairs[BIAS_ROW:BIAS_ROW + 1, ZC - 1, :], 1.0).then_inc(pads_zero, 1)
            mark(1)
            for m in range(2, NP):
                mark(m)
                if m - 2 < NG:
                    group_copies(0, [m - 2])
                if m == 2:
                    dve.wait_ge(w1d_in, 32)
                    nc.vector.tensor_tensor(w1d[:, 0, :], w1d[:, 0, :], w1d[:, 1, :],
                                            AluOpType.add).then_inc(w1d_added, 1)
            for n in range(len(W1_PIECES)):
                w1_rest(n)
            group_copies(0, range(NP - 2, NG))
            dense_rest(0)
            with dve.Fori(0, TILES - 1) as t:
                pair_copies(t)
                group_copies(t + 1, AFTER_PRODUCTS)
                group_copies(t + 1, AFTER_LAYER1)
                group_copies(t + 1, AFTER_HIDDEN)
                dense_rest(t + 1)
                output(t)
            pair_copies(TILES - 1)
            output(TILES - 1)

        @block.scalar
        def _(act):
            def upper(m):
                k = m % 2
                act.wait_ge(table_in[k], 32 * (m // 2 + 1))
                if m >= 2:
                    act.wait_ge(picked, m - 1)
                nc.scalar.copy(hi[:, k, :, :], raw[:, k, :, :]).then_inc(hi_ready, 1)
                act.wait_ge(idb_in[k], 16 * (m // 2 + 1))
                if m > 0:
                    act.wait_ge(marked_act, ACT_LOTS * m)
                for c in range(DVE_LOTS, LOTS):
                    nc.scalar.activation(distance[:, c - DVE_LOTS, :], idb[0:SHARE, k, :], ACT.Abs,
                                         bias=minus_rowid[0:SHARE, c:c + 1]).then_inc(distance_ready, 1)
                for c in range(DVE_LOTS, LOTS):
                    act.wait_ge(distance_ready, ACT_LOTS * m + c - DVE_LOTS + 1)
                    nc.scalar.activation(onehot[:, k, c, :], distance[:, c - DVE_LOTS, :], ACT.Relu,
                                         bias=1.0, scale=-1.0).then_inc(marked_act, 1)

            def w1_upper(n):
                c = parts(W1_PIECES[n])
                act.wait_ge(w1z_in[n], 16 * (len(slots_of(n)) + (n == len(W1_PIECES) - 1)))
                nc.scalar.copy(wzhi[:, c, :], w1z[:, c, :]).then_inc(w1_hi, 1)
                if n == len(W1_PIECES) - 1:
                    act.wait_ge(w1d_added, 1)
                    nc.scalar.copy(wdhi[:, :], w1d[:, 0, :]).then_inc(w1_hi, 1)

            def keep(m):
                act.wait_ge(picked, m + 1)
                nc.scalar.copy(whole[:, 1 + m, :], picked_acc[m % 2]).then_inc(kept, 1)

            def spread_whole(t):
                at = 0
                for run in WHOLE_RUNS:
                    last = nc.scalar.copy(vecT[:, :, :, span(run)].rearrange("p k s v -> p v s k"),
                                          whole[:, at:at + len(run), bass.ds(t * TB, TB)]
                                          .rearrange("p v (s k) -> p v s k", k=Q))
                    at += len(run)
                last.then_inc(spread, 1)

            def dense_upper(t):
                nc.scalar.copy(dhi[:, :], whole[:, 0, bass.ds(t * TB, TB)]).then_inc(dhi_ready, 1)

            def group_copies(t, groups):
                for g in groups:
                    if g % 2 == 1:
                        act.wait_ge(turn_done, t * NG + g + 1)
                        vec_copy(nc.scalar.copy, g).then_inc(vec_act, 1)

            def pair_copies(t):
                for n in range(GRAMS):
                    act.wait_ge(gram_done, t * GRAMS + n + 1)
                    pairs_copy(nc.scalar.copy, 2, n)
                    pairs_copy(nc.scalar.copy, 3, n).then_inc(pairs_act, 1)
                act.wait_ge(pairs_dve, t * GRAMS + GRAMS)
                act.wait_ge(pairs_act, t * GRAMS + GRAMS)
                for c in (slice(0, ZHALF), slice(ZHALF, ZC)):
                    nc.scalar.copy(phi[:, c, :], pairs[:, c, :]).then_inc(phi_ready, 1)

            def hidden(t):
                act.wait_ge(h1_done, t + 1)
                for half in range(2):
                    n = slice(half * C1 // 2, (half + 1) * C1 // 2)
                    nc.scalar.activation(h1[:, n, :], h1p[:, :].rearrange("b (n k) -> b n k", k=128)[:, n, :],
                                         ACT.Relu).then_inc(h1_ready, 1)

            def hidden_turned(t):
                act.wait_ge(h1T_done, t + 1)
                nc.scalar.copy(h1T[:, :, :], h1Tp[:, :, :]).then_inc(h1T_ready, 1)

            act.wait_ge(rowid_ready, 1)
            nc.scalar.mul(minus_rowid[:, :], rowid[:, :], -1.0).then_inc(minus_ready, 1)
            act.wait_ge(minus_ready, 1)
            upper(0)
            upper(1)
            for m in range(NP):
                keep(m)
                if m == 0:
                    act.wait_ge(dense_turned, 1)
                    nc.scalar.copy(whole[:, 0, :], turned[1][:, :, :].rearrange("p a b -> p (a b)")
                                   ).then_inc(dense_kept, 1)
                if m + 2 < NP:
                    upper(m + 2)
                if m == NP - 3:
                    w1_upper(0)
                    w1_upper(1)
                if m == NP - 2:
                    w1_upper(2)
                    w1_upper(3)
                if m >= 1 and m - 1 < NG:
                    group_copies(0, [m - 1])
            group_copies(0, range(NP - 1, NG))
            act.wait_ge(kept, NP)
            act.wait_ge(dense_kept, 1)
            act.wait_ge(pads_zero, 2)
            dense_upper(0)
            spread_whole(0)
            with act.Fori(0, TILES - 1) as t:
                pair_copies(t)
                spread_whole(t + 1)
                group_copies(t + 1, AFTER_PRODUCTS)
                hidden(t)
                dense_upper(t + 1)
                group_copies(t + 1, AFTER_LAYER1)
                hidden_turned(t)
                group_copies(t + 1, AFTER_HIDDEN)
            pair_copies(TILES - 1)
            hidden(TILES - 1)
            hidden_turned(TILES - 1)


INPUTS = (["r_dense_features", "ids"] + [f"tbl_{f}" for f in range(FIELDS)]
          + ["W_top1", "b_top1", "W_top2", "b_top2", "W_top3"])


def kernel(**inputs):
    import numpy as np
    import concourse.bacc as bacc
    from concourse import mybir
    from concourse.bass_utils import run_bass_kernel_spmd as run

    nc = bacc.Bacc("TRN2", target_bir_lowering=False, num_devices=1)
    arrays, ap = {}, {}
    for name in INPUTS:
        a = np.asarray(inputs[name])
        if name in ("b_top1", "b_top2", "W_top3"):
            a = a.reshape(1, -1)
        a = np.ascontiguousarray(a)
        arrays["in_" + name] = a
        ap[name] = nc.dram_tensor("in_" + name, a.shape, mybir.dt.from_np(a.dtype), kind="ExternalInput").ap()
    arrays["in_ids_by_field"] = np.ascontiguousarray(arrays["in_ids"].T)
    ids_by_field = nc.dram_tensor("in_ids_by_field", (FIELDS, BATCH), mybir.dt.int32, kind="ExternalInput").ap()
    out = nc.dram_tensor("out_y", (TB, TILES), mybir.dt.float32, kind="ExternalOutput").ap()
    dlrm_tower(nc, ap["r_dense_features"], ap["ids"], ids_by_field, [ap[f"tbl_{f}"] for f in range(FIELDS)],
               ap["W_top1"], ap["b_top1"], ap["W_top2"], ap["b_top2"], ap["W_top3"], out)
    r = run(nc, [arrays], core_ids=[0])
    return r.results[0]["out_y"].T.reshape(BATCH, 1)
```

```python
import concourse.bass as bass
from concourse import mybir
from concourse.alu_op_type import AluOpType
from contextlib import ExitStack

fp32 = mybir.dt.float32
fp32r = mybir.dt.float32r
i32 = mybir.dt.int32
ACT = mybir.ActivationFunctionType

BATCH, D, FIELDS = 512, 128, 26
NV = FIELDS + 1
TB = 128
TILES = BATCH // TB
N1, N2 = 512, 256
C1 = N1 // 128
QUADS, Q = 4, 32
SLOTS = NV - 1
ZC = -(-SLOTS // QUADS)
ZHALF = (ZC + 1) // 2
BIAS_ROW = Q * (SLOTS - QUADS * (ZC - 1))
GRP = 4
FOUR = Q * (QUADS - 1) + NV
VPAD = Q
SHARE = 125
PICKED_FIRST, PICKED_LATER = [8, 17, 18, 20, 25], [11, 13, 14]
PICKED = PICKED_FIRST + PICKED_LATER
NP, NF = len(PICKED), len(PICKED_FIRST)
ACT_LOTS = [0, 2, 2, 2, 1, 1, 1, 2]
BATCH_K = 8
GRAMS = TB // QUADS // BATCH_K
WARM_UP = 21


def runs(vectors):
    out = []
    for v in vectors:
        r = out[-1] if out else []
        if r and len(r) < GRP and (len(r) == 1 or v - r[-1] == r[1] - r[0]):
            r.append(v)
        else:
            out.append([v])
    return out


def span(run):
    return slice(run[0], run[-1] + 1, run[1] - run[0] if len(run) > 1 else 1)


GROUPS = [sorted(runs([v for v in range(1, NV) if v - 1 not in fields]), key=lambda group: -len(group))
          for fields in (PICKED_FIRST, PICKED)]
NG = len(GROUPS[0])
assert len(GROUPS[1]) == NG
EVEN, ODD = len(range(0, NG, 2)), len(range(1, NG, 2))
WHOLE = [0] + [f + 1 for f in PICKED]
WHOLE_RUNS = runs(WHOLE[:1 + NF]) + runs(WHOLE[1 + NF:])
FIRST_RUNS = len(runs(WHOLE[:1 + NF]))
AFTER_PRODUCTS, IN_LAYER1 = range(0, 2), [range(2, 4), range(4, NG)]
BEFORE = 6
FIRST_TURNS = [[], [0], [1], [2, 3], [4], []]
RING = 28


def groups(t):
    return GROUPS[min(t, 1)]


SEQUENCE = [(t, g, v) for t in range(TILES) for g, group in enumerate(groups(t)) for v in group]
GATHER_OF = {(t, v): n for n, (t, g, v) in enumerate(SEQUENCE)}


def place(t, v):
    return GATHER_OF[t, v] % RING


def last_turn(t, v):
    n = GATHER_OF[t, v] - RING
    return SEQUENCE[n][0] * NG + SEQUENCE[n][1] + 1 if n >= 0 else 0


def samples(m):
    return slice(0 if m < NF else TB, BATCH)


def pair_row(i):
    return D + i * (NV - 1) - i * (i - 1) // 2


def chunk_rows(c):
    return BIAS_ROW + 1 if c == ZC - 1 else 128


W1_PIECES = [range(c, min(c + 2, ZC)) for c in range(0, ZC, 2)]


def piece_of(i):
    return i // QUADS // len(W1_PIECES[0])


def slots_of(n):
    return range(QUADS * W1_PIECES[n][0], min(QUADS * (W1_PIECES[n][-1] + 1), SLOTS))


def dlrm_tower(nc, dense, ids, ids_by_field, tables, w1, b1, w2, b2, w3, out):
    LOTS = tables[PICKED[0]].shape[0] // SHARE
    DVE_LOTS = [LOTS - n for n in ACT_LOTS]
    for f in PICKED:
        assert LOTS * SHARE == tables[f].shape[0]

    with ExitStack() as ctx:
        def sb(name, shape, dt=fp32):
            return ctx.enter_context(nc.sbuf_tensor(name, shape, dt))

        def pb(name, shape):
            return ctx.enter_context(nc.psum_tensor(name, shape, fp32))

        def sem(name):
            return ctx.enter_context(nc.semaphore(name))

        idx = sb("idx", [TB, TILES, FIELDS], i32)
        idb = sb("idb", [128, 2, BATCH], i32)
        rowid = sb("rowid", [128, LOTS])
        minus_rowid = sb("minus_rowid", [128, LOTS])
        distance = sb("distance", [SHARE, max(ACT_LOTS), BATCH])
        raw = sb("raw", [SHARE, 2, LOTS, D])
        hi = sb("hi", [SHARE, 2, LOTS, D], fp32r)
        lo = sb("lo", [SHARE, 2, LOTS, D], fp32r)
        onehot = sb("onehot", [SHARE, 2, LOTS, BATCH], fp32r)
        whole = sb("whole", [D, 1 + NP, BATCH])
        drows = sb("drows", [TB, TILES, D])
        rows = sb("rows", [TB, RING, D])
        vecT = sb("vecT", [D, Q, QUADS, VPAD])
        dhi = sb("dhi", [D, TB], fp32r)
        dlo = sb("dlo", [D, TB], fp32r)
        pairs = sb("pairs", [128, ZC, TB])
        phi = sb("phi", [128, ZC, TB], fp32r)
        plo = sb("plo", [128, ZC, TB], fp32r)
        ident = sb("ident", [128, 128])
        w1d = sb("w1d", [D, 2, N1])
        wdhi = sb("wdhi", [D, N1], fp32r)
        wdlo = sb("wdlo", [D, N1], fp32r)
        w1z = sb("w1z", [128, ZC, N1])
        wzhi = sb("wzhi", [128, ZC, N1], fp32r)
        wzlo = sb("wzlo", [128, ZC, N1], fp32r)
        w2s = sb("w2s", [128, C1, N2])
        b2s = sb("b2s", [128, N2])
        w3s = sb("w3s", [128, N2])
        h1 = sb("h1", [TB, C1, 128])
        h1T = sb("h1T", [128, C1, TB])
        h2 = sb("h2", [TB, N2])
        weighted = sb("weighted", [TB, N2])
        y = sb("y", [TB, TILES])

        turned = [pb(f"turned{k}", [128, GRP, TB]) for k in range(2)]
        gram = [pb(f"gram{k}", [128, BATCH_K, 128]) for k in range(2)]
        picked_acc = [gram[k][:, 0:GRP, :].rearrange("p a b -> p (a b)") for k in range(2)]
        h1p = pb("h1p", [TB, N1])
        h1Tp = pb("h1Tp", [128, C1, TB])
        h2p = h1Tp[:, 0:N2 // TB, :].rearrange("p a b -> p (a b)")

        def flat(bank):
            return bank[:, 0:C1 // 2, :].rearrange("p a b -> p (a b)")

        last_h1p = [h1p[:, 0:N1 // 2], flat(gram[0])]
        last_h1Tp = [h1Tp[:, 0:C1 // 2, :], gram[1][:, 0:C1 // 2, :]]
        last_h2p = flat(turned[0])

        ids_in = sem("ids_in")
        idb_in = [sem(f"idb_in{k}") for k in range(2)]
        table_in = [sem(f"table_in{k}") for k in range(2)]
        dense_in = sem("dense_in")
        zeros_dve = sem("zeros_dve")
        zeros_act = sem("zeros_act")
        w1z_in = [sem(f"w1z_in{n}") for n in range(len(W1_PIECES))]
        w1d_in = sem("w1d_in")
        small_in = sem("small_in")
        gathered = [[sem(f"gathered{k}_{g}") for g in range(NG)] for k in range(2)]
        ident_zero = sem("ident_zero")
        ident_ready = sem("ident_ready")
        rowid_ready = sem("rowid_ready")
        pads_zero = sem("pads_zero")
        ones_ready = sem("ones_ready")
        w1d_added = sem("w1d_added")
        w1_hi = sem("w1_hi")
        w1_lo = sem("w1_lo")
        minus_ready = sem("minus_ready")
        distance_ready = sem("distance_ready")
        hi_ready = sem("hi_ready")
        lo_ready = sem("lo_ready")
        marked_dve = sem("marked_dve")
        marked_act = sem("marked_act")
        picked = sem("picked")
        dense_turned = sem("dense_turned")
        dense_kept = sem("dense_kept")
        kept = sem("kept")
        turn_done = sem("turn_done")
        vec_dve = sem("vec_dve")
        vec_act = sem("vec_act")
        spread = sem("spread")
        dhi_ready = sem("dhi_ready")
        dlo_ready = sem("dlo_ready")
        gram_done = sem("gram_done")
        pairs_dve = sem("pairs_dve")
        pairs_act = sem("pairs_act")
        phi_ready = sem("phi_ready")
        plo_ready = sem("plo_ready")
        h1_done = sem("h1_done")
        h1_ready = sem("h1_ready")
        h1T_done = sem("h1T_done")
        h1T_ready = sem("h1T_ready")
        h2_done = sem("h2_done")
        h2_ready = sem("h2_ready")
        y_ready = sem("y_ready")
        stored = sem("stored")
        block = ctx.enter_context(nc.Block())

        def parts(c):
            return slice(c[0], c[-1] + 1)

        @block.sync
        def _(sp):
            def load_table(m):
                f, k = PICKED[m], m % 2
                if m >= 2:
                    sp.wait_ge(lo_ready, m - 1)
                src = tables[f].rearrange("(p c) d -> p c d", c=LOTS)
                cut = SHARE - SHARE % 15
                for a, b in ((0, cut), (cut, SHARE)):
                    sp.dma_start(raw[a:b, k, :, :], src[a:b, :, :]).then_inc(table_in[k], 16)

            def load_ids(m):
                if m >= 2:
                    sp.wait_ge(marked_dve, sum(DVE_LOTS[:m - 1]))
                    if sum(ACT_LOTS[:m - 1]):
                        sp.wait_ge(marked_act, sum(ACT_LOTS[:m - 1]))
                f = PICKED[m]
                sp.dma_start(idb[:, m % 2, :],
                             ids_by_field[f:f + 1, :].to_broadcast([128, BATCH])).then_inc(idb_in[m % 2], 16)

            def load_w1z(a, b):
                for i in range(a, b):
                    p = Q * (i % QUADS)
                    sp.dma_start(w1z[p + i + 1:p + NV, i // QUADS, :],
                                 w1[pair_row(i):pair_row(i) + NV - 1 - i, :]).then_inc(w1z_in[piece_of(i)], 16)

            sp.dma_start(idx[:, :, :], ids.rearrange("(t p) f -> p t f", p=TB)).then_inc(ids_in, 16)
            load_ids(0)
            load_table(0)
            load_ids(1)
            load_table(1)
            sp.dma_start(drows[:, :, :], dense.rearrange("(t p) d -> p t d", p=TB)).then_inc(dense_in, 16)
            sp.wait_ge(zeros_dve, 1)
            sp.wait_ge(zeros_act, 1)
            load_w1z(0, 8)
            load_ids(2)
            load_table(2)
            load_w1z(8, 12)
            load_ids(3)
            load_table(3)
            sp.dma_start(w1d[:, 0, :], w1[0:D, :]).then_inc(w1d_in, 16)
            sp.dma_start(w1d[:, 1, :], w1[w1.shape[0] - D:, :]).then_inc(w1d_in, 16)
            load_w1z(12, 16)
            load_ids(4)
            load_table(4)
            load_w1z(16, 20)
            load_ids(5)
            load_table(5)
            load_w1z(20, SLOTS)
            sp.dma_start(w1z[BIAS_ROW:BIAS_ROW + 1, ZC - 1, :], b1).then_inc(w1z_in[-1], 16)
            for m in range(6, NP):
                load_ids(m)
                load_table(m)
            sp.dma_start(w2s[:, :, :], w2.rearrange("(c p) n -> p c n", p=128)).then_inc(small_in, 16)
            sp.dma_start(b2s[:, :], b2.to_broadcast([128, N2])).then_inc(small_in, 16)
            sp.dma_start(w3s[:, :], w3.to_broadcast([128, N2])).then_inc(small_in, 16)
            sp.wait_ge(y_ready, TILES)
            sp.dma_start(out, y[:, :]).then_inc(stored, 16)
            sp.wait_ge(stored, 16)

        @block.gpsimd
        def _(pool):
            nc.gpsimd.iota(rowid[:, :], pattern=[[1, LOTS]], base=0, channel_multiplier=LOTS,
                           allow_small_or_imprecise_dtypes=True).then_inc(rowid_ready, 1)
            nc.gpsimd.memset(ident[:, :], 0.0).then_inc(ident_zero, 1)
            pool.wait_ge(ident_zero, 1)
            nc.gpsimd.affine_select(out=ident[:, :], in_=ident[:, :], compare_op=AluOpType.not_equal, fill=1.0,
                                    base=0, pattern=[[-1, 128]], channel_multiplier=1).then_inc(ident_ready, 1)
            pool.wait_ge(ids_in, 16)
            for t in range(TILES):
                for g, group in enumerate(groups(t)):
                    for v in group:
                        if last_turn(t, v):
                            pool.wait_ge(turn_done, last_turn(t, v))
                        pool.indirect_dma_start(rows[:, place(t, v), :], None, tables[v - 1][:, :],
                                                bass.IndirectOffsetOnAxis(ap=idx[:, t, v - 1:v], axis=0)
                                                ).then_inc(gathered[t % 2][g], 16)

        @block.tensor
        def _(pe):
            def pick(m, group=None):
                k = m % 2
                if m >= 2:
                    pe.wait_ge(kept, m - 1)
                pe.wait_ge(hi_ready, m + 1)
                b = samples(m)
                for c in range(LOTS):
                    if c < DVE_LOTS[m]:
                        pe.wait_ge(marked_dve, sum(DVE_LOTS[:m]) + c + 1)
                    else:
                        pe.wait_ge(marked_act, sum(ACT_LOTS[:m]) + c - DVE_LOTS[m] + 1)
                    nc.tensor.matmul(picked_acc[k][:, b], hi[:, k, c, :], onehot[:, k, c, b], start=(c == 0), stop=False)
                if group is not None:
                    turn(0, group)
                pe.wait_ge(lo_ready, m + 1)
                for c in range(LOTS):
                    last = nc.tensor.matmul(picked_acc[k][:, b], lo[:, k, c, :], onehot[:, k, c, b],
                                            start=False, stop=(c == LOTS - 1))
                last.then_inc(picked, 1)

            def turn(t, g, free=True):
                group = groups(t)[g]
                pe.wait_ge(gathered[t % 2][g], 16 * sum(len(groups(n)[g]) for n in range(t % 2, t + 1, 2)))
                if free:
                    if g % 2 == 0:
                        pe.wait_ge(vec_dve, t * EVEN + g // 2)
                    else:
                        pe.wait_ge(vec_act, t * ODD + g // 2)
                for n, v in enumerate(group):
                    last = nc.tensor.transpose(turned[g % 2][:, n, :], rows[:, place(t, v), :], ident[:, :])
                last.then_inc(turn_done, 1)

            def products(t, hidden_before):
                pe.wait_ge(vec_dve, t * EVEN + EVEN)
                pe.wait_ge(vec_act, t * ODD + ODD)
                pe.wait_ge(spread, FIRST_RUNS + t * len(WHOLE_RUNS))
                for n in range(GRAMS):
                    if t == 0 and n < 2:
                        pe.wait_ge(kept, BEFORE - 1 + n)
                    if n >= 2:
                        pe.wait_ge(pairs_dve, t * GRAMS + n - 1)
                        pe.wait_ge(pairs_act, t * GRAMS + n - 1)
                    for k in range(BATCH_K):
                        four = vecT[:, n * BATCH_K + k, :, :]
                        last = nc.tensor.matmul(gram[n % 2][0:FOUR, k, 0:QUADS * SLOTS],
                                                four.rearrange("p s v -> p (s v)")[:, 0:FOUR],
                                                four[:, :, 0:SLOTS], start=True, stop=True)
                    last.then_inc(gram_done, 1)
                    if n == 1 and hidden_before:
                        turn_hidden(t - 1)

            def layer1(t, turns=((), ()), acc=h1p[:, :], cols=slice(0, N1), last_hidden=False):
                pe.wait_ge(dhi_ready, t + 1)
                pe.wait_ge(dlo_ready, t + 1)
                if t == 0:
                    pe.wait_ge(w1_hi, 1)
                    pe.wait_ge(w1_lo, 1)
                nc.tensor.matmul(acc, dhi[:, :], wdhi[:, cols], start=True, stop=False)
                nc.tensor.matmul(acc, dhi[:, :], wdlo[:, cols], start=False, stop=False)
                nc.tensor.matmul(acc, dlo[:, :], wdhi[:, cols], start=False, stop=False)
                for half, chunks in enumerate((range(ZHALF), range(ZHALF, ZC))):
                    if half == 1:
                        for g in turns[0]:
                            turn(t + 1, g)
                        if last_hidden:
                            turn_last_hidden(0)
                    pe.wait_ge(phi_ready, t * 2 + half + 1)
                    if t == 0:
                        pe.wait_ge(w1_hi, 1 + len(W1_PIECES) * (half + 1) // 2)
                        pe.wait_ge(w1_lo, 1 + len(W1_PIECES) * (half + 1) // 2)
                    for c in chunks:
                        k = chunk_rows(c)
                        nc.tensor.matmul(acc, phi[0:k, c, :], wzhi[0:k, c, cols], start=False, stop=False)
                        nc.tensor.matmul(acc, phi[0:k, c, :], wzlo[0:k, c, cols], start=False, stop=False)
                    if half == 1:
                        for g in turns[1]:
                            turn(t + 1, g)
                    pe.wait_ge(plo_ready, t * 2 + half + 1)
                    for c in chunks:
                        k = chunk_rows(c)
                        last = nc.tensor.matmul(acc, plo[0:k, c, :], wzhi[0:k, c, cols],
                                                start=False, stop=(c == ZC - 1))
                last.then_inc(h1_done, 1)

            def turn_hidden(t):
                for n in range(C1):
                    if n % (C1 // 2) == 0:
                        pe.wait_ge(h1_ready, t * 2 + n // (C1 // 2) + 1)
                    if n == 0 and t > 0:
                        pe.wait_ge(h2_ready, t)
                    last = nc.tensor.transpose(h1Tp[:, n, :], h1[:, n, :], ident[:, :])
                last.then_inc(h1T_done, 1)

            def turn_last_hidden(half):
                pe.wait_ge(h1_ready, (TILES - 1) * 2 + half + 1)
                if half == 0:
                    pe.wait_ge(h2_ready, TILES - 1)
                for n in range(C1 // 2):
                    last = nc.tensor.transpose(last_h1Tp[half][:, n, :], h1[:, half * C1 // 2 + n, :], ident[:, :])
                last.then_inc(h1T_done, 1)

            def last_layers():
                t = TILES - 1
                layer1(t, acc=last_h1p[0], cols=slice(0, N1 // 2))
                layer1(t, acc=last_h1p[1], cols=slice(N1 // 2, N1), last_hidden=True)
                nc.tensor.matmul(last_h2p, pairs[BIAS_ROW:BIAS_ROW + 1, ZC - 1, :], b2s[BIAS_ROW:BIAS_ROW + 1, :],
                                 start=True, stop=False)
                turn_last_hidden(1)
                for half in range(2):
                    pe.wait_ge(h1T_ready, t + half + 1)
                    for n in range(half * C1 // 2, (half + 1) * C1 // 2):
                        last = nc.tensor.matmul(last_h2p, h1T[:, n, :], w2s[:, n, :], start=False, stop=(n == C1 - 1))
                last.then_inc(h2_done, 1)

            def layer2(t):
                pe.wait_ge(h1T_ready, t + 1)
                if t == 0:
                    pe.wait_ge(small_in, 48)
                for n in range(C1):
                    last = nc.tensor.matmul(h2p, h1T[:, n, :], w2s[:, n, :], start=(n == 0), stop=(n == C1 - 1))
                last.then_inc(h2_done, 1)

            pe.wait_ge(ident_ready, 1)
            for n in range(WARM_UP):
                nc.tensor.transpose(h1Tp[:, n % C1, :], ident[:, :], ident[:, :])
            for m in range(BEFORE):
                pick(m, group=(NG - 1 if m == BEFORE - 1 else None))
                if m == 0:
                    pe.wait_ge(dense_in, 16)
                    for t in range(TILES):
                        last = nc.tensor.transpose(turned[1][:, t, :], drows[:, t, :], ident[:, :])
                    last.then_inc(dense_turned, 1)
                for g in FIRST_TURNS[m]:
                    if g == 1:
                        pe.wait_ge(dense_kept, 1)
                    turn(0, g, free=(g > 1))
            for t in range(TILES):
                more = t + 1 < TILES
                products(t, hidden_before=(0 < t < TILES - 1))
                if t == 0:
                    for m in range(BEFORE, NP):
                        pe.wait_ge(pairs_dve, GRAMS - 1 if m == BEFORE else GRAMS)
                        pe.wait_ge(pairs_act, GRAMS - 1 if m == BEFORE else GRAMS)
                        pick(m)
                        turn(1, AFTER_PRODUCTS[m - BEFORE])
                else:
                    for g in AFTER_PRODUCTS if more else ():
                        turn(t + 1, g)
                    layer2(t - 1)
                if t < TILES - 2:
                    layer1(t, IN_LAYER1)
                elif more:
                    layer1(t, [IN_LAYER1[0], IN_LAYER1[1][:-1]])
                    turn_hidden(t)
                    turn(t + 1, NG - 1)
            last_layers()

        def pairs_copy(copy, s, n):
            for jm in range(QUADS):
                slots = len(range(jm, SLOTS, QUADS))
                a = s * SLOTS + jm
                last = copy(pairs[jm * Q:jm * Q + NV, 0:slots, s * Q + n * BATCH_K:s * Q + (n + 1) * BATCH_K],
                            gram[n % 2][s * Q:s * Q + NV, :, a:a + (slots - 1) * QUADS + 1:QUADS]
                            .rearrange("p k c -> p c k"))
            return last

        def vec_copy(copy, group, g):
            return copy(vecT[:, :, :, span(group)].rearrange("p k s v -> p v s k"),
                        turned[g % 2][:, 0:len(group), :].rearrange("p v (s k) -> p v s k", k=Q))

        @block.vector
        def _(dve):
            def rest(out, whole_value, upper):
                return nc.vector.tensor_tensor(out, whole_value, upper.bitcast(fp32), AluOpType.subtract)

            def mark(m):
                k = m % 2
                dve.wait_ge(idb_in[k], 16 * (m // 2 + 1))
                if m >= 2:
                    dve.wait_ge(picked, m - 1)
                b = samples(m)
                for c in range(DVE_LOTS[m]):
                    nc.vector.tensor_scalar(onehot[:, k, c, b], idb[0:SHARE, k, b], rowid[0:SHARE, c:c + 1],
                                            None, AluOpType.is_equal).then_inc(marked_dve, 1)

            def table_rest(m):
                k = m % 2
                if m >= 2:
                    dve.wait_ge(picked, m - 1)
                dve.wait_ge(hi_ready, m + 1)
                rest(lo[:, k, :, :], raw[:, k, :, :], hi[:, k, :, :]).then_inc(lo_ready, 1)

            def w1d_sum():
                dve.wait_ge(w1d_in, 32)
                nc.vector.tensor_tensor(w1d[:, 0, :], w1d[:, 0, :], w1d[:, 1, :], AluOpType.add).then_inc(w1d_added, 1)

            def w1d_rest():
                dve.wait_ge(w1_hi, 1)
                rest(wdlo[:, :], w1d[:, 0, :], wdhi[:, :]).then_inc(w1_lo, 1)

            def w1_rest(n):
                c = parts(W1_PIECES[n])
                dve.wait_ge(w1_hi, n + 2)
                rest(wzlo[:, c, :], w1z[:, c, :], wzhi[:, c, :]).then_inc(w1_lo, 1)

            def group_copies(t, which, groups=GROUPS[1]):
                for g in which:
                    if g % 2 == 0:
                        dve.wait_ge(turn_done, t * NG + g + 1)
                        vec_copy(nc.vector.tensor_copy, groups[g], g).then_inc(vec_dve, 1)

            def batch_copies(t, n):
                dve.wait_ge(gram_done, t * GRAMS + n + 1)
                pairs_copy(nc.vector.tensor_copy, 0, n)
                pairs_copy(nc.vector.tensor_copy, 1, n).then_inc(pairs_dve, 1)

            def pairs_rest(t):
                for half, c in enumerate((slice(0, ZHALF), slice(ZHALF, ZC))):
                    dve.wait_ge(phi_ready, t * 2 + half + 1)
                    rest(plo[:, c, :], pairs[:, c, :], phi[:, c, :]).then_inc(plo_ready, 1)

            def dense_rest(t):
                dve.wait_ge(dhi_ready, t + 1)
                rest(dlo[:, :], whole[:, 0, bass.ds(t * TB, TB)], dhi[:, :]).then_inc(dlo_ready, 1)

            def output(t):
                dve.wait_ge(h2_done, t + 1)
                nc.vector.tensor_tensor(h2[:, :], h2p, b2s[:, :], AluOpType.add).then_inc(h2_ready, 1)
                dve.wait_ge(h2_ready, t + 1)
                nc.vector.scalar_tensor_tensor(weighted[:, :], h2[:, :], 0.0, w3s[:, :], AluOpType.max, AluOpType.mult,
                                               accum_out=y[:, bass.ds(t, 1)]).then_inc(y_ready, 1)

            nc.vector.memset(w1z[:, 0:ZHALF, :], 0.0).then_inc(zeros_dve, 1)
            dve.wait_ge(rowid_ready, 1)
            mark(0)
            table_rest(0)
            mark(1)
            table_rest(1)
            mark(2)
            table_rest(2)
            group_copies(0, [0], GROUPS[0])
            mark(3)
            table_rest(3)
            w1d_sum()
            mark(4)
            table_rest(4)
            group_copies(0, [2], GROUPS[0])
            mark(5)
            table_rest(5)
            group_copies(0, [4], GROUPS[0])
            w1d_rest()
            dense_rest(0)
            dve.wait_ge(pads_zero, 2)
            nc.vector.memset(pairs[BIAS_ROW:BIAS_ROW + 1, ZC - 1, :], 1.0).then_inc(ones_ready, 1)
            mark(6)
            batch_copies(0, 0)
            table_rest(6)
            batch_copies(0, 1)
            w1_rest(0)
            batch_copies(0, 2)
            batch_copies(0, 3)
            mark(7)
            table_rest(7)
            w1_rest(1)
            w1_rest(2)
            w1_rest(3)
            pairs_rest(0)
            with dve.Fori(0, TILES - 1) as t:
                group_copies(t + 1, range(NG))
                dense_rest(t + 1)
                for n in range(GRAMS):
                    batch_copies(t + 1, n)
                pairs_rest(t + 1)
                output(t)
            dve.wait_ge(y_ready, TILES - 1)
            dve.wait_ge(h2_done, TILES)
            nc.vector.scalar_tensor_tensor(weighted[:, :], last_h2p, 0.0, w3s[:, :], AluOpType.max, AluOpType.mult,
                                           accum_out=y[:, TILES - 1:TILES]).then_inc(y_ready, 1)

        @block.scalar
        def _(act):
            def upper(m):
                k = m % 2
                act.wait_ge(table_in[k], 32 * (m // 2 + 1))
                if m >= 2:
                    act.wait_ge(picked, m - 1)
                nc.scalar.copy(hi[:, k, :, :], raw[:, k, :, :]).then_inc(hi_ready, 1)
                act.wait_ge(idb_in[k], 16 * (m // 2 + 1))
                mine, before, b = range(DVE_LOTS[m], LOTS), sum(ACT_LOTS[:m]), samples(m)
                if before:
                    act.wait_ge(marked_act, before)
                for n, c in enumerate(mine):
                    nc.scalar.activation(distance[:, n, b], idb[0:SHARE, k, b], ACT.Abs,
                                         bias=minus_rowid[0:SHARE, c:c + 1]).then_inc(distance_ready, 1)
                for n, c in enumerate(mine):
                    act.wait_ge(distance_ready, before + n + 1)
                    nc.scalar.activation(onehot[:, k, c, b], distance[:, n, b], ACT.Relu,
                                         bias=1.0, scale=-1.0).then_inc(marked_act, 1)

            def w1d_upper():
                act.wait_ge(w1d_added, 1)
                nc.scalar.copy(wdhi[:, :], w1d[:, 0, :]).then_inc(w1_hi, 1)

            def w1_upper(n):
                c = parts(W1_PIECES[n])
                act.wait_ge(w1z_in[n], 16 * (len(slots_of(n)) + (n == len(W1_PIECES) - 1)))
                nc.scalar.copy(wzhi[:, c, :], w1z[:, c, :]).then_inc(w1_hi, 1)

            def keep(m):
                act.wait_ge(picked, m + 1)
                nc.scalar.copy(whole[:, 1 + m, samples(m)], picked_acc[m % 2][:, samples(m)]).then_inc(kept, 1)

            def spread_whole(t, which=range(len(WHOLE_RUNS))):
                for n in which:
                    run, at = WHOLE_RUNS[n], sum(len(r) for r in WHOLE_RUNS[:n])
                    nc.scalar.copy(vecT[:, :, :, span(run)].rearrange("p k s v -> p v s k"),
                                   whole[:, at:at + len(run), bass.ds(t * TB, TB)]
                                   .rearrange("p v (s k) -> p v s k", k=Q)).then_inc(spread, 1)

            def dense_upper(t):
                nc.scalar.copy(dhi[:, :], whole[:, 0, bass.ds(t * TB, TB)]).then_inc(dhi_ready, 1)

            def group_copies(t, which, groups=GROUPS[1]):
                for g in which:
                    if g % 2 == 1:
                        act.wait_ge(turn_done, t * NG + g + 1)
                        vec_copy(nc.scalar.copy, groups[g], g).then_inc(vec_act, 1)

            def batch_copies(t, n):
                act.wait_ge(gram_done, t * GRAMS + n + 1)
                pairs_copy(nc.scalar.copy, 2, n)
                pairs_copy(nc.scalar.copy, 3, n).then_inc(pairs_act, 1)

            def pairs_upper(t):
                act.wait_ge(pairs_dve, t * GRAMS + GRAMS)
                act.wait_ge(pairs_act, t * GRAMS + GRAMS)
                for c in (slice(0, ZHALF), slice(ZHALF, ZC)):
                    nc.scalar.copy(phi[:, c, :], pairs[:, c, :]).then_inc(phi_ready, 1)

            def hidden(t):
                act.wait_ge(h1_done, t + 1)
                for half in range(2):
                    n = slice(half * C1 // 2, (half + 1) * C1 // 2)
                    nc.scalar.activation(h1[:, n, :], h1p[:, :].rearrange("b (n k) -> b n k", k=128)[:, n, :],
                                         ACT.Relu).then_inc(h1_ready, 1)

            def hidden_turned(t):
                act.wait_ge(h1T_done, t + 1)
                nc.scalar.copy(h1T[:, :, :], h1Tp[:, :, :]).then_inc(h1T_ready, 1)

            act.wait_ge(rowid_ready, 1)
            nc.scalar.mul(minus_rowid[:, :], rowid[:, :], -1.0).then_inc(minus_ready, 1)
            act.wait_ge(zeros_dve, 1)
            nc.scalar.copy(w1z[:, ZHALF:ZC, :], w1z[:, 0:ZC - ZHALF, :]).then_inc(zeros_act, 1)
            act.wait_ge(minus_ready, 1)
            act.wait_ge(ident_ready, 1)
            nc.scalar.mul(vecT[:, :, :, NV:VPAD].rearrange("p k s v -> p (k s) v"),
                          ident[:, :].unsqueeze(2).to_broadcast([128, 128, VPAD - NV]), 0.0).then_inc(pads_zero, 1)
            upper(0)
            nc.scalar.mul(pairs[:, :, :], ident[:, :].unsqueeze(1).to_broadcast([128, ZC, 128]), 0.0
                          ).then_inc(pads_zero, 1)
            upper(1)
            keep(0)
            act.wait_ge(dense_turned, 1)
            nc.scalar.copy(whole[:, 0, :], turned[1][:, :, :].rearrange("p a b -> p (a b)")).then_inc(dense_kept, 1)
            upper(2)
            keep(1)
            upper(3)
            keep(2)
            group_copies(0, [1], GROUPS[0])
            upper(4)
            keep(3)
            group_copies(0, [3], GROUPS[0])
            w1d_upper()
            upper(5)
            act.wait_ge(dense_kept, 1)
            dense_upper(0)
            keep(4)
            act.wait_ge(kept, NF)
            act.wait_ge(pads_zero, 2)
            spread_whole(0, range(FIRST_RUNS))
            group_copies(0, [5], GROUPS[0])
            keep(5)
            upper(6)
            act.wait_ge(ones_ready, 1)
            batch_copies(0, 0)
            batch_copies(0, 1)
            w1_upper(0)
            batch_copies(0, 2)
            w1_upper(1)
            batch_copies(0, 3)
            upper(7)
            pairs_upper(0)
            keep(6)
            w1_upper(2)
            w1_upper(3)
            keep(7)
            act.wait_ge(kept, NP)
            with act.Fori(0, TILES - 2) as t:
                spread_whole(t + 1)
                group_copies(t + 1, AFTER_PRODUCTS)
                group_copies(t + 1, IN_LAYER1[0])
                group_copies(t + 1, IN_LAYER1[1])
                hidden(t)
                dense_upper(t + 1)
                batch_copies(t + 1, 0)
                batch_copies(t + 1, 1)
                hidden_turned(t)
                batch_copies(t + 1, 2)
                batch_copies(t + 1, 3)
                pairs_upper(t + 1)
            t = TILES - 2
            spread_whole(t + 1)
            group_copies(t + 1, range(NG - 1))
            hidden(t)
            dense_upper(t + 1)
            group_copies(t + 1, [NG - 1])
            hidden_turned(t)
            for n in range(GRAMS):
                batch_copies(t + 1, n)
            pairs_upper(t + 1)
            for half in range(2):
                n = slice(half * C1 // 2, (half + 1) * C1 // 2)
                act.wait_ge(h1_done, TILES + half)
                nc.scalar.activation(h1[:, n, :], last_h1p[half].rearrange("b (n k) -> b n k", k=128),
                                     ACT.Relu).then_inc(h1_ready, 1)
                act.wait_ge(h1T_done, TILES + half)
                nc.scalar.copy(h1T[:, n, :], last_h1Tp[half]).then_inc(h1T_ready, 1)


INPUTS = (["r_dense_features", "ids"] + [f"tbl_{f}" for f in range(FIELDS)]
          + ["W_top1", "b_top1", "W_top2", "b_top2", "W_top3"])


def kernel(**inputs):
    import numpy as np
    import concourse.bacc as bacc
    from concourse import mybir
    from concourse.bass_utils import run_bass_kernel_spmd as run

    nc = bacc.Bacc("TRN2", target_bir_lowering=False, num_devices=1)
    arrays, ap = {}, {}
    for name in INPUTS:
        a = np.asarray(inputs[name])
        if name in ("b_top1", "b_top2", "W_top3"):
            a = a.reshape(1, -1)
        a = np.ascontiguousarray(a)
        arrays["in_" + name] = a
        ap[name] = nc.dram_tensor("in_" + name, a.shape, mybir.dt.from_np(a.dtype), kind="ExternalInput").ap()
    arrays["in_ids_by_field"] = np.ascontiguousarray(arrays["in_ids"].T)
    ids_by_field = nc.dram_tensor("in_ids_by_field", (FIELDS, BATCH), mybir.dt.int32, kind="ExternalInput").ap()
    out = nc.dram_tensor("out_y", (TB, TILES), mybir.dt.float32, kind="ExternalOutput").ap()
    dlrm_tower(nc, ap["r_dense_features"], ap["ids"], ids_by_field, [ap[f"tbl_{f}"] for f in range(FIELDS)],
               ap["W_top1"], ap["b_top1"], ap["W_top2"], ap["b_top2"], ap["W_top3"], out)
    r = run(nc, [arrays], core_ids=[0])
    return r.results[0]["out_y"].T.reshape(BATCH, 1)
```
